# Optimizing a Trainium2 kernel written in Bass

```python
import numpy as np
import jax
import jax.numpy as jnp

def _softmax(x, axis=-1):
    return jax.nn.softmax(x, axis=axis)

def _gelu(x):
    return jax.nn.gelu(x, approximate=True)

def _silu(x):
    return jax.nn.silu(x)

def _sigmoid(x):
    return jax.nn.sigmoid(x)

def _layernorm(x, axis=-1, eps=1e-05):
    m = jnp.mean(x, axis=axis, keepdims=True)
    v = jnp.var(x, axis=axis, keepdims=True)
    return (x - m) / jnp.sqrt(v + eps)

def _scatter_add(tgt, idx, src, axis=0):
    return tgt.at[idx].add(src)

def _segment_sum(src, seg, n):
    return jax.ops.segment_sum(src, seg, n)
kernel_name = 'mk_early_fusion_d1_tok_img1024_r4_9510da'

def setup_inputs(seed: int=0):
    np.random.seed(seed)
    _w = jnp.asarray

    def _rec_inputs():
        import jax
        import jax.numpy as jnp
        _rk = jax.random.key(seed)
        x = -0.000356955 + 1 * jax.random.normal(jax.random.fold_in(_rk, 1), (16, 3, 96, 96), jnp.float32)
        txt = 8.02234e-05 + 0.554281 * jax.random.normal(jax.random.fold_in(_rk, 2), (16, 128, 256), jnp.float32)
        return (x, txt)
    x, txt = _rec_inputs()

    def _L0_tok_setup():
        import jax, jax.numpy as jnp
        import numpy as np
        PATCH = 16
        EMBED = 256
        key = jax.random.key(seed)
        kx, kw = jax.random.split(key, 2)
        x = jax.random.normal(kx, (128, 3, 224, 224), dtype=jnp.float32)
        in_feat = PATCH * PATCH * 3
        W = jax.random.normal(kw, (EMBED, in_feat), dtype=jnp.float32) * 0.02
        b = jnp.zeros((EMBED,), dtype=jnp.float32)
        return {'x': x, 'W': W, 'b': b}
    _L0_tok_all = _L0_tok_setup()
    _L0_tok_in = {k: v for k, v in _L0_tok_all.items() if k in ('W', 'b')}
    del _L0_tok_all

    def _L0_attn_setup():
        import math
        import jax, jax.numpy as jnp
        import numpy as np
        B, S, E, H = (4, 512, 256, 16)
        HD = E // H
        key = jax.random.key(seed)
        ks = jax.random.split(key, 7)
        scale = 1.0 / math.sqrt(E)
        return {'x': jax.random.normal(ks[0], (B, S, E), dtype=jnp.float32), 'Wq': jax.random.normal(ks[1], (H, HD, E), dtype=jnp.float32) * scale, 'bq': jax.random.normal(ks[2], (H, HD), dtype=jnp.float32) * 0.01, 'Wk': jax.random.normal(ks[3], (H, HD, E), dtype=jnp.float32) * scale, 'bk': jax.random.normal(ks[4], (H, HD), dtype=jnp.float32) * 0.01, 'Wv': jax.random.normal(ks[5], (H, HD, E), dtype=jnp.float32) * scale, 'bv': jax.random.normal(ks[6], (H, HD), dtype=jnp.float32) * 0.01}
    _L0_attn_all = _L0_attn_setup()
    _L0_attn_in = {k: v for k, v in _L0_attn_all.items() if k in ('Wq', 'bq', 'Wk', 'bk', 'Wv', 'bv')}
    del _L0_attn_all

    def _L0_ffn_setup():
        import jax, jax.numpy as jnp
        import numpy as np
        N_EMBD = 256
        EXPERT_SIZES = [(4, 256), (4, 512)]
        TOP_K = 2
        B, S = (1, 512)
        WIDTHS = []
        for count, size in EXPERT_SIZES:
            WIDTHS += [size] * count
        OFFSETS = np.concatenate([[0], np.cumsum(WIDTHS)]).astype(np.int64)
        E = len(WIDTHS)
        TOTAL_W = int(OFFSETS[-1])
        MAX_W = max(WIDTHS)

        def _stack_experts(w1, w2):
            W1e, W2e = ([], [])
            for e in range(E):
                off, wd = (int(OFFSETS[e]), WIDTHS[e])
                pad = MAX_W - wd
                W1e.append(jnp.pad(w1[:, off:off + wd], ((0, 0), (0, pad))))
                W2e.append(jnp.pad(w2[off:off + wd, :], ((0, pad), (0, 0))))
            return (jnp.stack(W1e), jnp.stack(W2e))
        key = jax.random.key(seed)
        k1, k2, k3, k4 = jax.random.split(key, 4)
        x = jax.random.normal(k1, (B, S, N_EMBD), jnp.float32)
        router_w = jax.random.normal(k2, (E, N_EMBD), jnp.float32) * 0.02
        w1 = jax.random.truncated_normal(k3, -3.0, 3.0, (N_EMBD, TOTAL_W), jnp.float32) * 0.02
        w2 = jax.random.truncated_normal(k4, -3.0, 3.0, (TOTAL_W, N_EMBD), jnp.float32) * 0.02
        return {'x': x, 'router_w': router_w, 'w1': w1, 'w2': w2}
    _L0_ffn_all = _L0_ffn_setup()
    _L0_ffn_in = {k: v for k, v in _L0_ffn_all.items() if k in ('router_w', 'w1', 'w2')}
    del _L0_ffn_all
    return {'x': x, 'txt': txt, 'L0_tok_W': _L0_tok_in['W'], 'L0_tok_b': _L0_tok_in['b'], 'L0_attn_Wq': _L0_attn_in['Wq'], 'L0_attn_bq': _L0_attn_in['bq'], 'L0_attn_Wk': _L0_attn_in['Wk'], 'L0_attn_bk': _L0_attn_in['bk'], 'L0_attn_Wv': _L0_attn_in['Wv'], 'L0_attn_bv': _L0_attn_in['bv'], 'L0_ffn_router_w': _L0_ffn_in['router_w'], 'L0_ffn_w1': _L0_ffn_in['w1'], 'L0_ffn_w2': _L0_ffn_in['w2']}

def reference(x, txt, L0_tok_W, L0_tok_b, L0_attn_Wq, L0_attn_bq, L0_attn_Wk, L0_attn_bk, L0_attn_Wv, L0_attn_bv, L0_ffn_router_w, L0_ffn_w1, L0_ffn_w2):
    import jax
    import jax.numpy as jnp

    def _L0_tok_ref(x, W, b):
        import jax, jax.numpy as jnp
        import numpy as np
        PATCH = 16
        EMBED = 256
        p = PATCH
        B, C, H, Wd = x.shape
        gh, gw = (H // p, Wd // p)
        patches = x.reshape(B, C, gh, p, gw, p).transpose(0, 1, 2, 4, 3, 5)
        patches = patches.reshape(B, gh * gw, p * p * C)
        return jnp.einsum('bnk,ek->bne', patches, W) + b

    def _L0_attn_ref(x, Wq, bq, Wk, bk, Wv, bv):
        import math
        import jax, jax.numpy as jnp
        import numpy as np
        B, S, E, H = (4, 512, 256, 16)
        HD = E // H
        b, s, e = x.shape
        h, hd, _ = Wq.shape
        inv_scale = 1.0 / math.sqrt(hd)
        q = jnp.einsum('bse,hde->bshd', x, Wq) + bq
        k = jnp.einsum('bse,hde->bshd', x, Wk) + bk
        v = jnp.einsum('bse,hde->bshd', x, Wv) + bv
        mask = jnp.triu(jnp.full((s, s), -jnp.inf, dtype=x.dtype), k=1)
        scores = (jnp.einsum('bqhd,bkhd->bhqk', q, k) + mask) * inv_scale
        attn = jax.nn.softmax(scores, axis=-1)
        out = jnp.einsum('bhqk,bkhd->bqhd', attn, v)
        return out.reshape(b, s, h * hd)

    def _L0_ffn_ref(x, router_w, w1, w2):
        import jax, jax.numpy as jnp
        import numpy as np
        N_EMBD = 256
        EXPERT_SIZES = [(4, 256), (4, 512)]
        TOP_K = 2
        B, S = (1, 512)
        WIDTHS = []
        for count, size in EXPERT_SIZES:
            WIDTHS += [size] * count
        OFFSETS = np.concatenate([[0], np.cumsum(WIDTHS)]).astype(np.int64)
        E = len(WIDTHS)
        TOTAL_W = int(OFFSETS[-1])
        MAX_W = max(WIDTHS)

        def _stack_experts(w1, w2):
            W1e, W2e = ([], [])
            for e in range(E):
                off, wd = (int(OFFSETS[e]), WIDTHS[e])
                pad = MAX_W - wd
                W1e.append(jnp.pad(w1[:, off:off + wd], ((0, 0), (0, pad))))
                W2e.append(jnp.pad(w2[off:off + wd, :], ((0, pad), (0, 0))))
            return (jnp.stack(W1e), jnp.stack(W2e))
        b, s, d = x.shape
        xf = x.reshape(-1, d)
        logits = xf @ router_w.T
        probs = jax.nn.sigmoid(logits.astype(jnp.float32))
        topw, sel = jax.lax.top_k(probs, TOP_K)
        topw = topw / (topw.sum(-1, keepdims=True) + 1e-20)
        topw = topw.astype(x.dtype)
        onehot = sel[:, :, None] == jnp.arange(E)[None, None, :]
        combine = jnp.sum(topw[:, :, None] * onehot, axis=1)
        W1e, W2e = _stack_experts(w1, w2)
        h = jnp.einsum('td,edw->tew', xf, W1e)
        h = jnp.square(jax.nn.relu(h))
        y = jnp.einsum('tew,ewd->ted', h, W2e)
        out = jnp.einsum('ted,te->td', y, combine)
        return out.reshape(b, s, d)
    h = _L0_tok_ref(x, L0_tok_W, L0_tok_b)
    h = jnp.concatenate([h, txt], axis=1)
    h = h + _L0_attn_ref(_layernorm(h, axis=-1), L0_attn_Wq, L0_attn_bq, L0_attn_Wk, L0_attn_bk, L0_attn_Wv, L0_attn_bv)
    h = h + _L0_ffn_ref(_layernorm(h, axis=-1), L0_ffn_router_w, L0_ffn_w1, L0_ffn_w2)
    return h

_drawn_inputs = setup_inputs


def setup_inputs(seed=0):
    import zlib

    import numpy as np

    out = dict(_drawn_inputs(seed))
    spreads = {'L0_tok_b': (0.0, 0.1)}
    factors = {'L0_attn_bq': 8.0, 'L0_attn_bk': 8.0, 'L0_attn_bv': 3.087}
    for name, (base, spread) in spreads.items():
        noise = np.random.default_rng([zlib.crc32(name.encode()), seed]).standard_normal(out[name].shape)
        drawn = base * np.exp(spread * noise) if base else spread * noise
        out[name] = jnp.asarray(drawn.astype(out[name].dtype))
    for name, factor in factors.items():
        out[name] = (out[name] * factor).astype(out[name].dtype)
    return out
```

```python
from contextlib import ExitStack

import numpy as np
import concourse.bass as bass
from concourse import mybir

F32 = mybir.dt.float32
BF16 = mybir.dt.bfloat16
I32 = mybir.dt.int32
U32 = mybir.dt.uint32
ACT = mybir.ActivationFunctionType
ALU = mybir.AluOpType
AX = mybir.AxisListType

P = 128
BATCH, CHANNELS, IMAGE, PATCH = 16, 3, 96, 16
PATCHES = (IMAGE // PATCH) ** 2
FEATS = CHANNELS * PATCH * PATCH
TEXT, EMBED = 128, 256
SEQ = PATCHES + TEXT
HEADS, HD = 16, 16
TOKENS = BATCH * SEQ
IMG_TOKENS = BATCH * PATCHES
EPS = 1e-5
TAIL = SEQ - P
PAIRS = BATCH // 2
W2 = 2 * SEQ
FC = FEATS // P
KC = EMBED // P
TOK_TILES = -(-IMG_TOKENS // P)
MASKED = -1e30
SCALE = HD ** -0.5
Q_PARTS = (0, 0, 1, 1, 0, 2)
K_PARTS = (0, 1, 0, 1, 2, 0)
ROWS = 16 * len(Q_PARTS)
SHIFT = ROWS + 2
HEADS_A, HEADS_T, HEADS_B = 4, 3, 8
UNITS_A = HEADS // HEADS_A
UNITS_T = -(-HEADS // HEADS_T)
UNITS_B = HEADS // HEADS_B
TAILQ = SEQ - 64
VW = 32

NARROW, WIDE, EXPERTS, UNIT = 256, 512, 8, 256
WIDTH = 4 * NARROW + 4 * WIDE
ZERO_OFF = WIDTH
TOPK = 2
GROUPS = 4 * PAIRS
SLOT_TILES = (TOKENS * TOPK) // P + EXPERTS - 1
RING = 8

AHEAD = 5


def upto(i, n):
    return min(n, HEADS - i * n)


def weave(a, b):
    out = []
    for n, x in enumerate(a):
        out += b[n * len(b) // len(a):(n + 1) * len(b) // len(a)] + [x]
    return out if a else list(b)


def pe_order():
    order = [("TOK", m) for m in range(TOK_TILES)]
    order += [("LNA", 0, 1), ("LNB", 0, 1), ("HB", 0)]
    for i in range(PAIRS + 3):
        scores, rest = [], []
        if 0 <= i - 1 < PAIRS:
            t = i - 1
            scores = [("SA", t, b, g) for b in range(2) for g in range(UNITS_A)]
            scores += [("SB", t, g) for g in range(UNITS_T)]
        now, late, last = i < PAIRS, 0 <= i - 2 < PAIRS, 0 <= i - 3 < PAIRS
        if last:
            rest += [("LNB", i - 3, 2), ("STORE", i - 3)]
        if 1 <= i < PAIRS - 1:
            rest += [("HT", i + 1)]
        if now:
            rest += [("T1", i, k) for k in range(KC)]
        project = []
        if now:
            for side in range(2):
                project += [("QKV", i, 2 * side), ("QKV", i, 2 * side + 1), ("PARTS", i, side)]
        exps = [[], []]
        if late:
            for b in range(2):
                exps[b] = [("STA", i - 2, b, g) for g in range(UNITS_T)] + [("STB", i - 2, b, g) for g in range(UNITS_B)]
        rest += weave(project, exps[0])
        between = []
        if i + 1 < PAIRS:
            between += [("LNA", i + 1, 1)]
        if last:
            between += [("T2", i - 3, k) for k in range(KC)] + [("R", i - 3)]
        if late:
            between += [("PV", i - 2, 0, q) for q in range(2)]
        if now:
            between += [("V", i, 0)]
        rest += weave(between, exps[1])
        if now:
            rest += [("RST", i, 0), ("RST", i, 1)]
        if late:
            rest += [("OTR", i - 2, 0, 0), ("OTR", i - 2, 0, 1)]
        if i + 1 < PAIRS:
            rest += [("LNB", i + 1, 1), ("HB", i + 1)]
        if late:
            rest += [("PV", i - 2, 1, q) for q in range(2)]
        if now:
            rest += [("V", i, 1)]
        if late:
            rest += [("OTR", i - 2, 1, 0), ("OTR", i - 2, 1, 1), ("LNA", i - 2, 2)]
        cut = len(rest) - 3 if scores else len(rest)
        merged = weave(rest[:cut], scores) + ([("MT", i - 1), ("MROW", i - 1)] if scores else []) + rest[cut:]
        order += merged
    return order


class Uses:

    def __init__(self, order, kinds):
        self.at = {s: n for n, s in enumerate(x for x in order if x[0] in kinds)}

    def bank(self, s):
        return self.at[s] % 2

    def before(self, s):
        return self.at[s] // 2

    def through(self, s):
        return self.at[s] // 2 + 1


def build(nc, patches_t, txt, w_tok, b_tok, w_qkv, b_q, b_k, b_v, w_router, w_1, w_2, out):
    order = pe_order()
    gen = Uses(order, ("TOK", "T1", "QKV", "V", "MT", "OTR", "T2", "R"))
    sc = Uses(order, ("SA", "SB"))
    st = Uses(order, ("STA", "STB"))
    himg = nc.dram_tensor("himg", [IMG_TOKENS, EMBED], F32).ap()
    xs = nc.dram_tensor("xs", [TOKENS, EMBED], F32).ap()

    with ExitStack() as ctx:
        def sb(name, shape, dt=F32, to=ctx):
            return to.enter_context(nc.sbuf_tensor(name, shape, dt))

        def sem(name):
            return ctx.enter_context(nc.semaphore(name))

        banks = {n: [ctx.enter_context(nc.psum_tensor(f"{n}{i}", [P, 512], F32)) for i in range(2)]
                 for n in ("gen", "score", "scoret", "o")}
        psG, psS, psT, psO = (banks[n] for n in ("gen", "score", "scoret", "o"))

        w1 = sb("w1", [P, KC, WIDTH + UNIT])
        w2 = sb("w2", [P, (WIDTH + UNIT) // P, EMBED])
        ident = sb("ident", [P, P])
        identb = sb("identb", [P, P], BF16)
        logits = sb("logits", [P, GROUPS, EXPERTS])
        ld_w = sem("ld_w"); ld_tok = sem("ld_tok"); ld_ffn = sem("ld_ffn")
        img_out = sem("img_out")
        consts = sem("consts")
        vones = sem("vones")
        gready = [sem(f"gready{i}") for i in range(2)]; gfree = [sem(f"gfree{i}") for i in range(2)]
        sready = [sem(f"sready{i}") for i in range(2)]; sfree = [sem(f"sfree{i}") for i in range(2)]
        tready = [sem(f"tready{i}") for i in range(2)]; tfree = [sem(f"tfree{i}") for i in range(2)]
        oready = [sem(f"oready{i}") for i in range(2)]; ofree = [sem(f"ofree{i}") for i in range(2)]
        ht_ld = [sem(f"ht_ld{i}") for i in range(4)]
        stacked = [sem(f"stacked{i}") for i in range(2)]
        mrow = [sem(f"mrow{i}") for i in range(2)]
        stored = [sem(f"stored{i}") for i in range(2)]
        mv_ready = sem("mv_ready"); rstd_ready = sem("rstd_ready"); xn_ready = sem("xn_ready"); xn2_ready = sem("xn2_ready")
        hb_ready = sem("hb_ready")
        part1 = sem("part1"); part2 = sem("part2"); parts_ready = sem("parts_ready")
        masked = sem("masked")
        dch = sem("dch"); pch = sem("pch")

        with ExitStack() as att:
            Qs = [sb(f"Qs{i}", [P, HEADS, W2], BF16, att) for i in range(2)]
            Ks = [sb(f"Ks{i}", [P, HEADS, W2], BF16, att) for i in range(2)]
            wqkv = sb("wqkv", [P, KC, 3 * EMBED], F32, att)
            wr = sb("wr", [P, KC, EXPERTS], F32, att)
            bq = sb("bq", [P, 2], F32, att)
            bk = sb("bk", [P, 2], F32, att)
            bv = sb("bv", [P, EMBED], F32, att)
            bt = sb("bt", [P, EMBED], F32, att)
            mask_a = sb("mask_a", [P, HEADS_A, P], BF16, att)
            mask_b = sb("mask_b", [P, HEADS_T, SEQ], BF16, att)
            ht = [sb(f"ht{i}", [P, 4, EMBED], F32, att) for i in range(4)]
            xn = [sb(f"xn{i}", [P, 4, EMBED], F32, att) for i in range(2)]
            xn2 = [sb(f"xn2{i}", [P, 4, EMBED], F32, att) for i in range(2)]
            xT = [sb(f"xT{i}", [P, KC, W2], F32, att) for i in range(2)]
            x2T = sb("x2T", [P, KC, W2], F32, att)
            parts = sb("parts", [P, 3, 4, W2], BF16, att)
            rest_ = [sb(f"rest{i}", [P, W2], F32, att) for i in range(2)]
            pta = [sb(f"pta{i}", [P, HEADS, SEQ], F32, att) for i in range(2)]
            ptb = [sb(f"ptb{i}", [TAIL, HEADS, TAIL], F32, att) for i in range(2)]
            vA = [sb(f"vA{i}", [P, 2, HEADS, VW], F32, att) for i in range(2)]
            vB = [sb(f"vB{i}", [TAIL, 2, HEADS, VW], F32, att) for i in range(2)]
            oT = [sb(f"oT{i}", [P, 4, SEQ], F32, att) for i in range(2)]
            on = sb("on", [P, HEADS, HD], F32, att)
            rc = sb("rc", [P, HEADS], F32, att)
            mx = [sb(f"mx{i}", [P, 3, HEADS], F32, att) for i in range(2)]
            mhi = [sb(f"mhi{i}", [HEADS, W2], BF16, att) for i in range(2)]
            mlo = [sb(f"mlo{i}", [HEADS, W2], BF16, att) for i in range(2)]
            st6 = sb("st6", [P, 4, 6], F32, att)
            mv = [sb(f"mv{i}", [P, 4, 2], F32, att) for i in range(2)]
            ve = sb("ve", [P, 4], F32, att)
            half = sb("half", [P, 4], F32, att)
            rstd = [sb(f"rstd{i}", [P, 4], F32, att) for i in range(2)]
            pta_flat = [x[:, :, :].rearrange("p h s -> p (h s)") for x in pta]
            pa = [pta_flat[c // 4][:, (c % 4) * IMG_TOKENS:(c % 4 + 1) * IMG_TOKENS] for c in range(FC)]
            wt = [ht[2 + c // 4][:, c % 4, :] for c in range(FC)]
            himg_s = [xn2[i][:, 0, :] for i in range(2)]

            block = att.enter_context(nc.Block())

            @block.sync
            def _(sp):
                for c in range(FC):
                    sp.dma_start(pa[c], patches_t[c * P:(c + 1) * P, :]).then_inc(ld_tok, 16)
                    sp.dma_start(wt[c], w_tok[c * P:(c + 1) * P, :]).then_inc(ld_tok, 16)
                sp.dma_start(bt[:, :], b_tok.to_broadcast([P, EMBED])).then_inc(ld_tok, 16)
                sp.dma_start(wqkv[:, :, :], w_qkv.rearrange("(k p) n -> p k n", p=P)).then_inc(ld_w, 16)
                sp.dma_start(bq[:, :], b_q).then_inc(ld_w, 16)
                sp.dma_start(bk[:, :], b_k).then_inc(ld_w, 16)
                sp.dma_start(bv[:, :], b_v.to_broadcast([P, EMBED])).then_inc(ld_w, 16)
                sp.dma_start(wr[:, :, :], w_router.rearrange("(k p) n -> p k n", p=P)).then_inc(ld_w, 16)

                def load_h(t):
                    if t >= 4:
                        sp.wait_ge(xn2_ready, t - 3)
                        sp.wait_ge(stored[t % 2], 64 * ((t - 4) // 2 + 1))
                    x, s = ht[t % 4], ht_ld[t % 4]
                    sp.dma_start(x[PATCHES:P, 0:2, :], txt[2 * t:2 * t + 2, 0:P - PATCHES, :].rearrange("b p d -> p b d")).then_inc(s, 16)
                    sp.dma_start(x[0:TAIL, 2:4, :], txt[2 * t:2 * t + 2, P - PATCHES:TEXT, :].rearrange("b p d -> p b d")).then_inc(s, 16)
                    sp.dma_start(x[0:PATCHES, 0:2, :], himg[2 * t * PATCHES:(2 * t + 2) * PATCHES, :].rearrange("(b p) d -> p b d", b=2)).then_inc(s, 16)

                for s in order:
                    if s[0] == "TOK":
                        m = s[1]
                        n = min(P, IMG_TOKENS - m * P)
                        sp.wait_ge(gfree[gen.bank(s)], gen.through(s))
                        sp.dma_start(himg[m * P:m * P + n, :], himg_s[m % 2][0:n, :]).then_inc(img_out, 16)
                        sp.wait_ge(img_out, 16 * (m + 1))
                        if m == TOK_TILES - 1:
                            load_h(0)
                            load_h(1)
                            sp.dma_start(w1[:, :, 0:WIDTH], w_1.rearrange("(k p) n -> p k n", p=P)).then_inc(ld_ffn, 16)
                            sp.dma_start(w2[:, 0:WIDTH // P, :], w_2.rearrange("(j p) n -> p j n", p=P)).then_inc(ld_ffn, 16)
                    if s[0] == "HT":
                        load_h(s[1])
                    if s[0] == "RST":
                        t, side = s[1:]
                        sp.wait_ge(parts_ready, 4 * t + 2 * side + 2)
                        if t >= 2:
                            for x in (("STB", t - 2, 1, UNITS_B - 2), ("STB", t - 2, 1, UNITS_B - 1)):
                                sp.wait_ge(tready[st.bank(x)], st.through(x))
                        dst, use = ((Qs, Q_PARTS), (Ks, K_PARTS))[side]
                        for j, part in enumerate(use):
                            sp.dma_start(dst[t % 2][16 * j:16 * j + 16, :, :],
                                         parts[:, part, 2 * side:2 * side + 2, :]).then_inc(stacked[t % 2], 16)
                    if s[0] == "MROW":
                        t = s[1]
                        sp.wait_ge(gfree[gen.bank(("MT", t))], gen.through(("MT", t)))
                        sp.dma_start(Qs[t % 2][ROWS:ROWS + 1, :, :], mhi[t % 2][:, :]).then_inc(mrow[t % 2], 16)
                        sp.dma_start(Qs[t % 2][ROWS + 1:ROWS + 2, :, :], mlo[t % 2][:, :]).then_inc(mrow[t % 2], 16)
                    if s[0] == "STORE":
                        t = s[1]
                        sp.wait_ge(xn2_ready, t + 1)
                        for d, x in ((out, ht[t % 4]), (xs, xn2[t % 2])):
                            v = d[2 * t * SEQ:(2 * t + 2) * SEQ, :].rearrange("(b s) d -> s b d", b=2)
                            sp.dma_start(v[0:P, :, :], x[:, 0:2, :]).then_inc(stored[t % 2], 16)
                            sp.dma_start(v[P:SEQ, :, :], x[0:TAIL, 2:4, :]).then_inc(stored[t % 2], 16)

                for i in range(2):
                    sp.wait_ge(stored[i], 64 * PAIRS // 2)
                sp.wait_ge(ld_ffn, 32)

            @block.gpsimd
            def _(pool):
                g = nc.gpsimd
                made = 0

                def const(ins):
                    nonlocal made
                    made += 1
                    ins.then_inc(consts, 1)
                    pool.wait_ge(consts, made)

                const(g.memset(ident[:, :], 1.0))
                const(g.affine_select(out=ident[:, :], in_=ident[:, :], compare_op=ALU.is_equal, fill=0.0,
                                      base=0, pattern=[[-1, P]], channel_multiplier=1))
                const(g.tensor_copy(identb[:, :], ident[:, :]))
                const(g.memset(half[:, :], -0.5))
                const(g.memset(mask_a[:, :, :], 0.0))
                const(g.affine_select(out=mask_a[:, :, :], in_=mask_a[:, :, :], compare_op=ALU.is_ge, fill=MASKED,
                                      base=0, pattern=[[0, HEADS_A], [-1, P]], channel_multiplier=1))
                const(g.memset(mask_b[:, :, :], 0.0))
                for h in range(2):
                    const(g.affine_select(out=mask_b[64 * h:64 * h + 64, :, :], in_=mask_b[64 * h:64 * h + 64, :, :],
                                          compare_op=ALU.is_ge, fill=MASKED, base=TAILQ,
                                          pattern=[[0, HEADS_T], [-1, SEQ]], channel_multiplier=1))
                for i in range(2):
                    const(g.memset(Ks[i][ROWS:SHIFT, :, :], 1.0))
                assert made == CONSTS

                chain = 0
                for s in order:
                    if s[0] == "LNA":
                        t, which = s[1:]
                        n = ln_at[s]
                        pool.wait_ge(mv_ready, n + 1)
                        g.tensor_scalar(ve[:, :], mv[n % 2][:, :, 1], EPS, None, ALU.add).then_inc(pch, 1)
                        chain += 1
                        pool.wait_ge(pch, chain)
                        g.tensor_tensor(rstd[n % 2][:, :], ve[:, :], half[:, :], ALU.pow).then_inc(rstd_ready, 1)
                    if s[0] == "HB":
                        t = s[1]
                        pool.wait_ge(xn_ready, t + 1)
                        pool.wait_ge(ld_w, 16 * 5)
                        h = ht[t % 4]
                        bias = bv[:, :].unsqueeze(1)
                        g.tensor_tensor(h[:, 0:2, :], h[:, 0:2, :], bias.to_broadcast([P, 2, EMBED]), ALU.add)
                        g.tensor_tensor(h[0:TAIL, 2:4, :], h[0:TAIL, 2:4, :], bias[0:TAIL].to_broadcast([TAIL, 2, EMBED]),
                                        ALU.add).then_inc(hb_ready, 1)
                    if s[0] == "PARTS":
                        t, side = s[1:]
                        for m in (2 * side, 2 * side + 1):
                            pool.wait_ge(part2, 4 * t + m + 1)
                            g.tensor_tensor(parts[:, 2, m, :], rest_[m % 2][:, :], parts[:, 1, m, :],
                                            ALU.subtract).then_inc(parts_ready, 1)
                    if s[0] in ("STA", "STB"):
                        t, b, u = s[1:]
                        pool.wait_ge(tfree[st.bank(s)], st.through(s))
                        if s[0] == "STA":
                            n = upto(u, HEADS_T)
                            x = pta[b][:, HEADS_T * u:HEADS_T * u + n, 0:P]
                            pat = [[0, n], [1, P]]
                        else:
                            n = HEADS_B
                            x = ptb[b][:, n * u:n * u + n, :]
                            pat = [[0, n], [1, TAIL]]
                        g.affine_select(out=x, in_=x, compare_op=ALU.is_ge, fill=0.0, base=0, pattern=pat,
                                        channel_multiplier=-1).then_inc(masked, 1)

            @block.scalar
            def _(act):
                a = nc.scalar
                act.wait_ge(ld_w, 16 * 5)
                for s in order:
                    if s[0] == "T1":
                        t, k = s[1:]
                        act.wait_ge(gready[gen.bank(s)], gen.through(s))
                        a.copy(xT[t % 2][:, k, :], psG[gen.bank(s)][:, 0:W2]).then_inc(gfree[gen.bank(s)], 1)
                    if s[0] == "T2":
                        t, k = s[1:]
                        act.wait_ge(gready[gen.bank(s)], gen.through(s))
                        if t >= 1:
                            x = ("R", t - 1)
                            act.wait_ge(gready[gen.bank(x)], gen.through(x))
                        a.copy(x2T[:, k, :], psG[gen.bank(s)][:, 0:W2]).then_inc(gfree[gen.bank(s)], 1)
                    if s[0] == "QKV":
                        t, m = s[1:]
                        act.wait_ge(gready[gen.bank(s)], gen.through(s))
                        if t >= 1:
                            act.wait_ge(stacked[(t - 1) % 2], 16 * 12 * ((t - 1) // 2 + 1))
                        bias = (bq, bk)[m // 2][:, m % 2:m % 2 + 1]
                        a.activation(parts[:, 0, m, :], psG[gen.bank(s)][:, 0:W2], ACT.Identity,
                                     bias=bias).then_inc(part1, 1)
                    if s[0] == "PARTS":
                        t, side = s[1:]
                        for m in (2 * side, 2 * side + 1):
                            x = ("QKV", t, m)
                            act.wait_ge(gfree[gen.bank(x)], gen.through(x))
                            a.copy(parts[:, 1, m, :], rest_[m % 2][:, :]).then_inc(part2, 1)
                    if s[0] == "V":
                        t, b = s[1:]
                        if t < 2 and b == 0:
                            act.wait_ge(vones, 8)
                        act.wait_ge(gready[gen.bank(s)], gen.through(s))
                        if t >= 2:
                            for q in range(2):
                                act.wait_ge(oready[q], 2 * (t - 2) + b + 1)
                        v = psG[gen.bank(s)][:, :].rearrange("p (w h d) -> p w h d", w=2, d=HD)
                        a.copy(vA[t % 2][:, b, :, 0:HD], v[:, 0])
                        a.copy(vB[t % 2][:, b, :, 0:HD], v[0:TAIL, 1]).then_inc(gfree[gen.bank(s)], 1)
                    if s[0] in ("STA", "STB"):
                        t, b, u = s[1:]
                        act.wait_ge(tready[st.bank(s)], st.through(s))
                        if t >= 1 and s[0] == "STA" and u == 0:
                            for q in range(2):
                                act.wait_ge(oready[q], 2 * (t - 1) + b + 1)
                        if s[0] == "STA":
                            n = upto(u, HEADS_T)
                            dst = pta[b][:, HEADS_T * u:HEADS_T * u + n, :]
                            src = psT[st.bank(s)][:, 0:n * SEQ].rearrange("p (h s) -> p h s", s=SEQ)
                        else:
                            dst = ptb[b][:, HEADS_B * u:HEADS_B * u + HEADS_B, :]
                            src = psT[st.bank(s)][0:TAIL, 0:HEADS_B * TAIL].rearrange("p (h s) -> p h s", s=TAIL)
                        a.activation(dst, src, ACT.Exp, scale=SCALE).then_inc(tfree[st.bank(s)], 1)
                    if s[0] == "PV":
                        t, b, q = s[1:]
                        act.wait_ge(oready[q], 2 * t + b + 1)
                        if t >= 1:
                            for half_ in range(2):
                                x = ("OTR", t - 1, b, half_)
                                act.wait_ge(gready[gen.bank(x)], gen.through(x))
                        a.copy(oT[b][:, 2 * q:2 * q + 2, :], psO[q][:, 0:W2].rearrange("p (g s) -> p g s", g=2)).then_inc(ofree[q], 1)

            @block.vector
            def _(dve):
                v = nc.vector
                chain = 0

                def link(ins):
                    nonlocal chain
                    chain += 1
                    ins.then_inc(dch, 1)
                    dve.wait_ge(dch, chain)

                for i in range(2):
                    v.memset(vA[i][:, :, :, HD + 1:VW], 0.0).then_inc(vones, 1)
                    v.memset(vB[i][:, :, :, HD + 1:VW], 0.0).then_inc(vones, 1)
                    v.memset(vA[i][:, :, :, HD:HD + 1], 1.0).then_inc(vones, 1)
                    v.memset(vB[i][:, :, :, HD:HD + 1], 1.0).then_inc(vones, 1)
                    link(v.memset(mv[i][:, :, :], 1.0))
                link(v.memset(logits[:, :, :], 0.0))
                for s in order:
                    if s[0] == "TOK":
                        m = s[1]
                        n = min(P, IMG_TOKENS - m * P)
                        if m >= 2:
                            dve.wait_ge(img_out, 16 * (m - 1))
                        dve.wait_ge(gready[gen.bank(s)], gen.through(s))
                        v.tensor_tensor(himg_s[m % 2][0:n, :], psG[gen.bank(s)][0:n, 0:EMBED], bt[0:n, :],
                                        ALU.add).then_inc(gfree[gen.bank(s)], 1)
                    if s[0] == "LNA":
                        t, which = s[1:]
                        n = ln_at[s]
                        h = ht[t % 4]
                        if which == 1:
                            dve.wait_ge(ht_ld[t % 4], 48 * (t // 4 + 1))
                        for c in range(4):
                            r = P if c < 2 else TAIL
                            ins = v.bn_stats(st6[0:r, c, :], h[0:r, c, :])
                            if c == 3:
                                link(ins)
                        if n >= 2:
                            dve.wait_ge(rstd_ready, n - 1)
                        for c in range(4):
                            r = P if c < 2 else TAIL
                            ins = v.bn_aggr(mv[n % 2][0:r, c, :], st6[0:r, c, :])
                        ins.then_inc(mv_ready, 1)
                    if s[0] == "LNB":
                        t, which = s[1:]
                        n = ln_at[("LNA", t, which)]
                        h = ht[t % 4]
                        dve.wait_ge(rstd_ready, n + 1)
                        dst, ready = ((xn, xn_ready), (xn2, xn2_ready))[which - 1]
                        if which == 1 and t >= 2:
                            for k in range(KC):
                                x = ("T1", t - 2, k)
                                dve.wait_ge(gready[gen.bank(x)], gen.through(x))
                        if which == 2:
                            if t < 2:
                                dve.wait_ge(img_out, 16 * TOK_TILES)
                            else:
                                dve.wait_ge(stored[t % 2], 64 * (t // 2))
                                for k in range(KC):
                                    x = ("T2", t - 2, k)
                                    dve.wait_ge(gready[gen.bank(x)], gen.through(x))
                        for c in range(4):
                            r = P if c < 2 else TAIL
                            ins = v.tensor_scalar(dst[t % 2][0:r, c, :], h[0:r, c, :], mv[n % 2][0:r, c, 0:1],
                                                  rstd[n % 2][0:r, c:c + 1], ALU.subtract, ALU.mult)
                        ins.then_inc(ready, 1)
                    if s[0] == "QKV":
                        t, m = s[1:]
                        dve.wait_ge(part1, 4 * t + m + 1)
                        if 4 * t + m >= 2:
                            dve.wait_ge(parts_ready, 4 * t + m - 1)
                        bias = (bq, bk)[m // 2][:, m % 2:m % 2 + 1]
                        v.scalar_tensor_tensor(out=rest_[m % 2][:, :], in0=psG[gen.bank(s)][:, 0:W2], scalar=bias,
                                               in1=parts[:, 0, m, :], op0=ALU.add,
                                               op1=ALU.subtract).then_inc(gfree[gen.bank(s)], 1)
                    if s[0] in ("SA", "SB"):
                        t = s[1]
                        dve.wait_ge(sready[sc.bank(s)], sc.through(s))
                        if s[0] == "SA":
                            b, u = s[2:]
                            src = psS[sc.bank(s)][:, :].rearrange("p (h s) -> p h s", s=P)
                            dst = mx[t % 2][:, b, HEADS_A * u:HEADS_A * (u + 1)]
                        else:
                            u = s[2]
                            n = upto(u, HEADS_T)
                            src = psS[sc.bank(s)][:, 0:n * SEQ].rearrange("p (h s) -> p h s", s=SEQ)
                            dst = mx[t % 2][:, 2, HEADS_T * u:HEADS_T * u + n]
                        v.tensor_reduce(dst, src, axis=AX.X, op=ALU.max).then_inc(sfree[sc.bank(s)], 1)
                    if s[0] == "MT":
                        t = s[1]
                        dve.wait_ge(gready[gen.bank(s)], gen.through(s))
                        if t >= 2:
                            dve.wait_ge(mrow[t % 2], 32 * (t // 2))
                        m0 = psG[gen.bank(s)][0:HEADS, 0:3 * P].rearrange("p (c s) -> p c s", s=P)
                        srcs = (m0[:, 0:2, :], m0[:, 2, :].rearrange("p (b s) -> p b s", b=2)[:, :, 64 - TAIL:64])
                        hi = mhi[t % 2][:, :].rearrange("p (b s) -> p b s", b=2)
                        lo = mlo[t % 2][:, :].rearrange("p (b s) -> p b s", b=2)
                        cut = (slice(0, P), slice(P, SEQ))
                        v.tensor_scalar(hi[:, :, cut[0]], srcs[0], -1.0, None, ALU.mult)
                        link(v.tensor_scalar(hi[:, :, cut[1]], srcs[1], -1.0, None, ALU.mult))
                        for x, c in zip(srcs, cut):
                            ins = v.scalar_tensor_tensor(out=lo[:, :, c], in0=x, scalar=-1.0, in1=hi[:, :, c],
                                                         op0=ALU.mult, op1=ALU.subtract)
                        ins.then_inc(gfree[gen.bank(s)], 1)
                    if s[0] == "OTR":
                        t, b, w = s[1:]
                        dve.wait_ge(gready[gen.bank(s)], gen.through(s))
                        dve.wait_ge(hb_ready, t + 1)
                        r = (P, TAIL)[w]
                        o = psG[gen.bank(s)][0:r, :].rearrange("p (h d) -> p h d", d=VW)
                        link(v.reciprocal(rc[0:r, :], o[:, :, HD]))
                        v.tensor_tensor(on[0:r, :, :], o[:, :, 0:HD], rc[0:r, :].unsqueeze(2).to_broadcast([r, HEADS, HD]),
                                        ALU.mult).then_inc(gfree[gen.bank(s)], 1)
                        dve.wait_ge(gfree[gen.bank(s)], gen.through(s))
                        h = ht[t % 4][0:r, 2 * w + b, :]
                        link(v.tensor_tensor(h, h, on[0:r, :, :].rearrange("p h d -> p (h d)"), ALU.add))
                    if s[0] == "R":
                        t = s[1]
                        dve.wait_ge(gready[gen.bank(s)], gen.through(s))
                        x = psG[gen.bank(s)][:, 0:4 * EXPERTS].rearrange("p (c e) -> p c e", e=EXPERTS)
                        v.tensor_copy(logits[:, 4 * t:4 * t + 2, :], x[:, 0:2, :])
                        v.tensor_copy(logits[0:TAIL, 4 * t + 2:4 * t + 4, :], x[0:TAIL, 2:4, :]).then_inc(gfree[gen.bank(s)], 1)

            @block.tensor
            def _(pe):
                mm = nc.tensor.matmul
                tr = nc.tensor.transpose
                pe.wait_ge(consts, CONSTS)

                def cols(c):
                    b, w = c % 2, c // 2
                    return b * SEQ + w * P, (P, TAIL)[w]

                for s in order:
                    if s in gen.at and gen.before(s):
                        pe.wait_ge(gfree[gen.bank(s)], gen.before(s))
                    if s in gen.at:
                        o = psG[gen.bank(s)]
                        done = gready[gen.bank(s)]
                    if s[0] == "TOK":
                        m = s[1]
                        n = min(P, IMG_TOKENS - m * P)
                        pe.wait_ge(ld_tok, 16 * (2 * FC + 1))
                        for c in range(FC):
                            ins = mm(o[0:n, 0:EMBED], pa[c][:, m * P:m * P + n], wt[c], start=c == 0, stop=c == FC - 1)
                        ins.then_inc(done, 1)
                    if s[0] in ("T1", "T2"):
                        t, k = s[1:]
                        src, ready = ((xn, xn_ready), (xn2, xn2_ready))[s[0] == "T2"]
                        pe.wait_ge(ready, t + 1)
                        for c in range(4):
                            at, r = cols(c)
                            ins = tr(o[:, at:at + r], src[t % 2][0:r, c, k * P:(k + 1) * P], ident[0:r, 0:r])
                        ins.then_inc(done, 1)
                    if s[0] == "QKV":
                        t, m = s[1:]
                        x = ("T1", t, KC - 1)
                        for k in range(KC):
                            x = ("T1", t, k)
                            pe.wait_ge(gfree[gen.bank(x)], gen.through(x))
                        if t == 0 and m == 0:
                            pe.wait_ge(ld_w, 16 * 5)
                        for k in range(KC):
                            ins = mm(o[:, 0:W2], wqkv[:, k, m * P:(m + 1) * P], xT[t % 2][:, k, :], start=k == 0, stop=k == KC - 1)
                        ins.then_inc(done, 1)
                    if s[0] == "V":
                        t, b = s[1:]
                        for w in range(2):
                            at, r = cols(2 * w + b)
                            for k in range(KC):
                                ins = mm(o[0:r, w * EMBED:(w + 1) * EMBED], xT[t % 2][:, k, at:at + r],
                                         wqkv[:, k, 2 * EMBED:3 * EMBED], start=k == 0, stop=k == KC - 1)
                        ins.then_inc(done, 1)
                    if s[0] in ("SA", "SB"):
                        t = s[1]
                        q, k_ = Qs[t % 2], Ks[t % 2]
                        if sc.before(s):
                            pe.wait_ge(sfree[sc.bank(s)], sc.before(s))
                        pe.wait_ge(stacked[t % 2], 16 * 12 * (t // 2 + 1))
                        o = psS[sc.bank(s)]
                        if s[0] == "SA":
                            b, u = s[2:]
                            mm(o[:, :], identb[:, :], mask_a[:, :, :].rearrange("p h s -> p (h s)"), start=True, stop=False)
                            for j in range(HEADS_A):
                                h = HEADS_A * u + j
                                ins = mm(o[:, j * P:(j + 1) * P], q[0:ROWS, h, b * SEQ:b * SEQ + P],
                                         k_[0:ROWS, h, b * SEQ:b * SEQ + P], start=False, stop=j == HEADS_A - 1)
                        else:
                            u = s[2]
                            n = upto(u, HEADS_T)
                            mm(o[:, 0:n * SEQ], identb[:, :], mask_b[:, 0:n, :].rearrange("p h s -> p (h s)"), start=True, stop=False)
                            for j in range(n):
                                for b in range(2):
                                    h = HEADS_T * u + j
                                    ins = mm(o[64 * b:64 * b + 64, j * SEQ:(j + 1) * SEQ],
                                             q[0:ROWS, h, b * SEQ + TAILQ:(b + 1) * SEQ],
                                             k_[0:ROWS, h, b * SEQ:(b + 1) * SEQ], start=False, stop=j == n - 1)
                        ins.then_inc(sready[sc.bank(s)], 1)
                    if s[0] == "MT":
                        t = s[1]
                        for x in (("SB", t, UNITS_T - 2), ("SB", t, UNITS_T - 1)):
                            pe.wait_ge(sfree[sc.bank(x)], sc.through(x))
                        for c in range(3):
                            ins = tr(o[0:HEADS, c * P:(c + 1) * P], mx[t % 2][:, c, :], ident[:, :])
                        ins.then_inc(done, 1)
                    if s[0] in ("STA", "STB"):
                        t, b, u = s[1:]
                        q, k_ = Qs[t % 2], Ks[t % 2]
                        pe.wait_ge(mrow[t % 2], 32 * (t // 2 + 1))
                        if st.before(s):
                            pe.wait_ge(tfree[st.bank(s)], st.before(s))
                        o = psT[st.bank(s)]
                        if s[0] == "STA":
                            for j in range(upto(u, HEADS_T)):
                                h = HEADS_T * u + j
                                ins = mm(o[:, j * SEQ:(j + 1) * SEQ], k_[0:SHIFT, h, b * SEQ:b * SEQ + P],
                                         q[0:SHIFT, h, b * SEQ:(b + 1) * SEQ], start=True, stop=True)
                        else:
                            for j in range(HEADS_B):
                                h = HEADS_B * u + j
                                ins = mm(o[0:TAIL, j * TAIL:(j + 1) * TAIL], k_[0:SHIFT, h, b * SEQ + P:(b + 1) * SEQ],
                                         q[0:SHIFT, h, b * SEQ + P:(b + 1) * SEQ], start=True, stop=True)
                        ins.then_inc(tready[st.bank(s)], 1)
                    if s[0] == "PV":
                        t, b, q = s[1:]
                        x = ("STB", t, b, UNITS_B - 1)
                        pe.wait_ge(masked, st.at[x] + 1)
                        x = ("V", t, b)
                        pe.wait_ge(gfree[gen.bank(x)], gen.through(x))
                        if 2 * t + b:
                            pe.wait_ge(ofree[q], 2 * t + b)
                        for g in range(2):
                            for j in range(4):
                                h = 8 * q + 4 * g + j
                                mm(psO[q][VW * j:VW * (j + 1), g * SEQ:(g + 1) * SEQ], vA[t % 2][:, b, h, :],
                                   pta[b][:, h, :], start=True, stop=False)
                            for j in range(4):
                                h = 8 * q + 4 * g + j
                                ins = mm(psO[q][VW * j:VW * (j + 1), g * SEQ + P:(g + 1) * SEQ], vB[t % 2][:, b, h, :],
                                         ptb[b][:, h, :], start=False, stop=True)
                        ins.then_inc(oready[q], 1)
                    if s[0] == "OTR":
                        t, b, w = s[1:]
                        for q in range(2):
                            pe.wait_ge(ofree[q], 2 * t + b + 1)
                        r = (P, TAIL)[w]
                        for g in range(4):
                            ins = tr(o[0:r, g * P:(g + 1) * P], oT[b][:, g, w * P:w * P + r], ident[:, :])
                        ins.then_inc(done, 1)
                    if s[0] == "R":
                        t = s[1]
                        for k in range(KC):
                            x = ("T2", t, k)
                            pe.wait_ge(gfree[gen.bank(x)], gen.through(x))
                        for c in range(4):
                            at, r = cols(c)
                            for k in range(KC):
                                ins = mm(o[0:r, c * EXPERTS:(c + 1) * EXPERTS], x2T[:, k, at:at + r], wr[:, k, :],
                                         start=k == 0, stop=k == KC - 1)
                        ins.then_inc(done, 1)

        with ExitStack() as ffn:
            dispatch_and_experts(nc, ctx, ffn, sb, sem, banks, w1, w2, ident, logits, xs, out)


def dispatch_and_experts(nc, ctx, ffn, sb, sem, banks, w1, w2, ident, logits, xs, out):
    psG, psS, psT, psO = (banks[n] for n in ("gen", "score", "scoret", "o"))
    E, G, S = EXPERTS, GROUPS, SLOT_TILES

    def f(name, shape, dt=F32):
        return sb(name, shape, dt, ffn)

    prob = f("prob", [P, E, G])
    left = f("left", [P, E, G])
    key = f("key", [P, E, G])
    hot = [f(f"hot{i}", [P, E, G]) for i in range(2)]
    sel = f("sel", [P, E, G])
    selb = f("selb", [P, E, G], BF16)
    top = [f(f"top{i}", [P, G]) for i in range(2)]
    best = f("best", [P, G])
    valid = f("valid", [P, G])
    nowhere = f("nowhere", [P, G])
    rev = f("rev", [P, E])
    token = f("token", [P, PAIRS, 2, 2])
    weight = [f(f"weight{i}", [P, G]) for i in range(2)]
    zeros = f("zeros", [P, E * G])
    ones_b = f("ones_b", [P, P], BF16)
    before_b = f("before_b", [P, P], BF16)
    total = f("total", [P, E, G])
    offset = f("offset", [P, E, G])
    held = f("held", [P, E])
    held_i = f("held_i", [P, E], I32)
    tiles_i = f("tiles_i", [P, E], I32)
    tiles = f("tiles", [P, E])
    tiles_end = f("tiles_end", [P, E])
    base = f("base", [P, E])
    slot = f("slot", [P, 2, G])
    slot_i = f("slot_i", [P, 2, G], I32)
    col_i = f("col_i", [P, 2, G], I32)
    row_i = f("row_i", [P, 2, G], I32)
    col = f("col", [P, 2, G])
    row = f("row", [P, 2, G])
    iota_r = f("iota_r", [P, P])
    iota_c = f("iota_c", [P, S])
    row_hot = [f(f"row_hot{i}", [P, P]) for i in range(4)]
    entry = [f(f"entry{i}", [P, 2, S]) for i in range(4)]
    dump = f("dump", [P, 1])
    pad = f("pad", [P, S])
    from_f = f("from_f", [P, S])
    to_f = f("to_f", [P, S])
    from_i = f("from_i", [P, S], U32)
    to_i = f("to_i", [P, S], U32)
    slot_w = f("slot_w", [P, S])
    which = f("which", [P, S, E])
    expert = f("expert", [P, S])
    over = f("over", [P, S])
    off = [f(f"off{i}", [P, S]) for i in range(2)]
    narrow = f("narrow", [P, S])
    off_i = f("off_i", [P, S, 2], I32)
    idx_from = [f(f"idx_from{i}", [P, 1], U32) for i in range(RING)]
    idx_to = [f(f"idx_to{i}", [P, 1], U32) for i in range(RING)]
    xg = [f(f"xg{i}", [P, EMBED]) for i in range(RING)]
    xgT = [f(f"xgT{i}", [P, KC, P]) for i in range(2)]
    hr = [f(f"hr{i}", [P, WIDE]) for i in range(2)]
    hT = [f(f"hT{i}", [P, WIDE // P, P]) for i in range(2)]
    ys = [f(f"ys{i}", [P, EMBED]) for i in range(2)]

    made = sem("made"); zeroed = sem("zeroed"); vch = sem("vch"); neg_exp = sem("neg_exp")
    selected = sem("selected"); counted = sem("counted"); pair_ready = sem("pair_ready"); pair_used = sem("pair_used")
    placed = sem("placed");
    taken_up = sem("taken_up"); idx_ready = sem("idx_ready"); gathered = [sem(f"gathered{i}") for i in range(RING)]
    x_t = sem("x_t"); x_c = sem("x_c"); h_mm = sem("h_mm"); h_c = sem("h_c"); h_t = sem("h_t"); h_sq = sem("h_sq")
    y_mm = sem("y_mm"); y_c = sem("y_c"); added = sem("added")
    loc = psG[0]; cnt = psG[1]; acc = psS[0]
    NPAIR = 2 * G

    def rolled(eng, lags, ahead):
        def slot_of(i, u):
            for stage, lag in lags:
                if not isinstance(i, int) or 0 <= i + lag < S:
                    stage(i + lag, (u + lag) % RING)

        for i in range(-ahead, RING):
            slot_of(i, i % RING)
        with eng.Fori(1, S // RING - 1, 1) as it:
            for u in range(RING):
                slot_of(it * RING + u, u)
        for i in range(S - RING, S + 1):
            slot_of(i, i % RING)

    with nc.Block() as block:
        @block.gpsimd
        def _(pool):
            g = nc.gpsimd
            n = 0

            def const(ins):
                nonlocal n
                n += 1
                ins.then_inc(made, 1)
                pool.wait_ge(made, n)

            const(g.iota(iota_r[:, :], pattern=[[1, P]], base=0, channel_multiplier=0, allow_small_or_imprecise_dtypes=True))
            const(g.iota(iota_c[:, :], pattern=[[1, S]], base=0, channel_multiplier=0, allow_small_or_imprecise_dtypes=True))
            const(g.iota(rev[:, :], pattern=[[-1, E]], base=E, channel_multiplier=0, allow_small_or_imprecise_dtypes=True))
            const(g.iota(token[:, :, :, :], pattern=[[2 * SEQ, PAIRS], [P, 2], [SEQ, 2]], base=1, channel_multiplier=1,
                         allow_small_or_imprecise_dtypes=True))
            const(g.iota(dump[:, :], pattern=[[0, 1]], base=TOKENS + 1, channel_multiplier=1, allow_small_or_imprecise_dtypes=True))
            const(g.memset(valid[:, :], 1.0))
            tails = valid[:, :].rearrange("p (t w b) -> p t w b", t=PAIRS, w=2)[:, :, 1, :]
            const(g.affine_select(out=tails, in_=tails, compare_op=ALU.is_gt, fill=0.0, base=TAIL,
                                  pattern=[[0, PAIRS], [0, 2]], channel_multiplier=-1))
            const(g.memset(zeros[:, :], 0.0))
            const(g.memset(ones_b[:, :], 1.0))
            const(g.affine_select(out=before_b[:, :], in_=ones_b[:, :], compare_op=ALU.is_gt, fill=0.0, base=0,
                                  pattern=[[1, P]], channel_multiplier=-1))
            const(g.memset(w1[:, :, WIDTH:], 0.0))
            const(g.memset(w2[:, WIDTH // P:, :], 0.0))
            assert n == MADE
            pool.dma_start(out[TOKENS:TOKENS + P, :], zeros[:, 0:EMBED]).then_inc(zeroed, 16)
            pool.wait_ge(zeroed, 16)

            last_token, last_row = pool.to_reg(TOKENS - 1), pool.to_reg(TOKENS + P - 1)

            def gather(i, r):
                pool.wait_ge(idx_ready, i + 1)
                pool.sem_inc(taken_up, 1)
                pool.indirect_dma_start(xg[r][:, :], None, xs, bass.IndirectOffsetOnAxis(ap=idx_from[r][:, 0:1], axis=0),
                                        bounds_check=last_token).then_inc(gathered[r], 16)

            def add(i, r):
                pool.wait_ge(y_c, i + 1)
                if not (isinstance(i, int) and i == 0):
                    pool.wait_ge(added, 16 * i)
                pool.sem_inc(taken_up, 1)
                pool.indirect_dma_start(out, bass.IndirectOffsetOnAxis(ap=idx_to[r][:, 0:1], axis=0), ys[r % 2][:, :], None,
                                        bounds_check=last_row, compute_op=ALU.add).then_inc(added, 16)

            rolled(pool, ((gather, AHEAD), (add, 0)), AHEAD)
            pool.wait_ge(added, 16 * S)

        @block.vector
        def _(dve):
            v = nc.vector
            chain = 0

            def link(ins):
                nonlocal chain
                chain += 1
                ins.then_inc(vch, 1)
                dve.wait_ge(vch, chain)

            def over_e(x):
                return x[:, :].unsqueeze(1).to_broadcast([P, E, G])

            def by_tile(x):
                return x[:, :, :].rearrange("p e c -> p c e")

            dve.wait_ge(made, MADE)
            dve.wait_ge(neg_exp, 1)
            link(v.tensor_scalar(left[:, :, :], prob[:, :, :], 1.0, None, ALU.add))
            link(v.reciprocal(prob[:, :, :], left[:, :, :]))
            revs = rev[:, :].unsqueeze(2).to_broadcast([P, E, G])
            src = prob
            for i in range(TOPK):
                link(v.tensor_reduce(top[i][:, :], by_tile(src), axis=AX.X, op=ALU.max))
                link(v.tensor_tensor(key[:, :, :], src[:, :, :], over_e(top[i]), ALU.is_equal))
                link(v.tensor_tensor(key[:, :, :], key[:, :, :], revs, ALU.mult))
                link(v.tensor_reduce(best[:, :], by_tile(key), axis=AX.X, op=ALU.max))
                link(v.tensor_tensor(hot[i][:, :, :], key[:, :, :], over_e(best), ALU.is_equal))
                if i == 0:
                    link(v.scalar_tensor_tensor(out=left[:, :, :], in0=hot[0][:, :, :], scalar=-4.0, in1=prob[:, :, :],
                                                op0=ALU.mult, op1=ALU.add))
                    src = left
            link(v.tensor_tensor(sel[:, :, :], hot[0][:, :, :], hot[1][:, :, :], ALU.add))
            v.tensor_tensor(selb[:, :, :], sel[:, :, :], over_e(valid), ALU.mult).then_inc(selected, 1)
            link(v.tensor_tensor(best[:, :], top[0][:, :], top[1][:, :], ALU.add))
            link(v.tensor_scalar(best[:, :], best[:, :], 1e-20, None, ALU.add))
            link(v.reciprocal(best[:, :], best[:, :]))
            for i in range(TOPK):
                link(v.tensor_tensor(weight[i][:, :], top[i][:, :], best[:, :], ALU.mult))
            link(v.tensor_scalar(nowhere[:, :], valid[:, :], -1.0, 1000.0, ALU.add, ALU.mult))
            dve.wait_ge(counted, 1)
            cnt3 = cnt[:, 0:E * G].rearrange("p (e c) -> p e c", e=E)
            link(v.tensor_tensor_scan(total[:, :, :].rearrange("p e c -> p (e c)"), cnt[:, 0:E * G], zeros[:, :], 0.0,
                                      op0=ALU.add, op1=ALU.add))
            link(v.tensor_tensor(offset[:, :, :], total[:, :, :], cnt3, ALU.subtract))
            link(v.tensor_tensor(held[:, :], total[:, :, G - 1], offset[:, :, 0], ALU.subtract))
            link(v.tensor_scalar(held_i[:, :], held[:, :], float(P - 1), None, ALU.add))
            link(v.tensor_scalar(tiles_i[:, :], held_i[:, :], 7, None, ALU.logical_shift_right))
            link(v.tensor_copy(tiles[:, :], tiles_i[:, :]))
            link(v.tensor_tensor_scan(tiles_end[:, :], tiles[:, :], zeros[:, 0:E], 0.0, op0=ALU.add, op1=ALU.add))
            link(v.tensor_tensor(base[:, :], tiles_end[:, :], tiles[:, :], ALU.subtract))
            link(v.scalar_tensor_tensor(out=base[:, :], in0=base[:, :], scalar=float(P), in1=offset[:, :, 0], op0=ALU.mult,
                                        op1=ALU.subtract))
            link(v.tensor_tensor(offset[:, :, :], offset[:, :, :], base[:, :].unsqueeze(2).to_broadcast([P, E, G]), ALU.add))
            link(v.tensor_tensor(offset[:, :, :], offset[:, :, :], loc[:, 0:E * G].rearrange("p (e c) -> p e c", e=E), ALU.add))
            for i in range(TOPK):
                link(v.tensor_tensor(key[:, :, :], offset[:, :, :], hot[i][:, :, :], ALU.mult))
                link(v.tensor_reduce(slot[:, i, :], by_tile(key), axis=AX.X, op=ALU.add))
            link(v.tensor_copy(slot_i[:, :, :], slot[:, :, :]))
            link(v.tensor_scalar(col_i[:, :, :], slot_i[:, :, :], 7, None, ALU.logical_shift_right))
            link(v.tensor_scalar(row_i[:, :, :], slot_i[:, :, :], P - 1, None, ALU.bitwise_and))
            link(v.tensor_copy(row[:, :, :], row_i[:, :, :]))
            link(v.tensor_copy(col[:, :, :], col_i[:, :, :]))
            link(v.tensor_tensor(col[:, :, :], col[:, :, :], nowhere[:, :].unsqueeze(1).to_broadcast([P, 2, G]), ALU.add))
            for n in range(NPAIR):
                i, c = n // G, n % G
                if n >= 4:
                    dve.wait_ge(pair_used, n - 3)
                v.tensor_scalar(row_hot[n % 4][:, :], iota_r[:, :], row[:, i, c:c + 1], None, ALU.is_equal)
                tok = token[:, :, :, :].rearrange("p t w b -> p (t w b)")
                v.tensor_scalar(entry[n % 4][:, 0, :], iota_c[:, :], col[:, i, c:c + 1], tok[:, c:c + 1], ALU.is_equal, ALU.mult)
                v.tensor_scalar(entry[n % 4][:, 1, :], iota_c[:, :], col[:, i, c:c + 1], weight[i][:, c:c + 1],
                                ALU.is_equal, ALU.mult).then_inc(pair_ready, 1)
            iota_s = iota_c[:, :].unsqueeze(2).to_broadcast([P, S, E])
            link(v.tensor_tensor(which[:, :, :], tiles_end[:, :].unsqueeze(1).to_broadcast([P, S, E]), iota_s, ALU.is_le))
            link(v.tensor_reduce(expert[:, :], which[:, :, :], axis=AX.X, op=ALU.add))
            link(v.tensor_scalar(expert[:, :], expert[:, :], float(E - 1), None, ALU.min))
            link(v.tensor_scalar(over[:, :], expert[:, :], -4.0, 0.0, ALU.add, ALU.max))
            link(v.tensor_tensor(over[:, :], over[:, :], expert[:, :], ALU.add))
            link(v.tensor_scalar(off[0][:, :], over[:, :], float(NARROW), None, ALU.mult))
            link(v.tensor_scalar(narrow[:, :], expert[:, :], 4.0, None, ALU.is_lt))
            link(v.tensor_scalar(off[1][:, :], off[0][:, :], -1.0, float(ZERO_OFF - UNIT), ALU.mult, ALU.add))
            link(v.tensor_tensor(off[1][:, :], off[1][:, :], narrow[:, :], ALU.mult))
            link(v.tensor_tensor(off[1][:, :], off[1][:, :], off[0][:, :], ALU.add))
            v.tensor_copy(off_i[:, :, 0], off[0][:, :])
            v.tensor_scalar(off_i[:, :, 1], off[1][:, :], float(UNIT), None, ALU.add).then_inc(placed, 1)
            dve.wait_ge(pair_used, NPAIR)
            link(v.tensor_scalar(pad[:, :], acc[:, 0:S], 0.0, None, ALU.is_equal))
            link(v.tensor_scalar(from_f[:, :], acc[:, 0:S], -1.0, 0.0, ALU.add, ALU.max))
            link(v.tensor_copy(from_i[:, :], from_f[:, :]))
            link(v.scalar_tensor_tensor(out=to_f[:, :], in0=pad[:, :], scalar=dump[:, 0:1], in1=acc[:, 0:S], op0=ALU.mult, op1=ALU.add))
            link(v.tensor_scalar(to_i[:, :], to_f[:, :], -1.0, None, ALU.add))
            link(v.tensor_copy(slot_w[:, :], acc[:, S:2 * S]))

            def indices(i, r):
                if not (isinstance(i, int) and i < RING):
                    dve.wait_ge(added, 16 * (i - RING + 1))
                v.tensor_copy(idx_from[r][:, :], from_i[:, bass.ds(i, 1)])
                v.tensor_copy(idx_to[r][:, :], to_i[:, bass.ds(i, 1)]).then_inc(idx_ready, 1)

            def result(i, r):
                dve.wait_ge(y_mm, i + 1)
                if not (isinstance(i, int) and i < 2):
                    dve.wait_ge(added, 16 * (i - 1))
                v.tensor_scalar(ys[r % 2][:, :], psO[r % 2][:, 0:EMBED], slot_w[:, bass.ds(i, 1)], None, ALU.mult).then_inc(y_c, 1)

            rolled(dve, ((indices, AHEAD), (result, 0)), AHEAD)

        @block.scalar
        def _(act):
            a = nc.scalar
            act.wait_ge(made, MADE)
            a.activation(prob[:, :, :], logits[:, :, :].rearrange("p c e -> p e c"), ACT.Exp, scale=-1.0).then_inc(neg_exp, 1)

            def x_copy(i, r):
                act.wait_ge(x_t, i + 1)
                if not (isinstance(i, int) and i < 2):
                    act.wait_ge(h_mm, i - 1)
                a.copy(xgT[r % 2][:, :, :], psG[r % 2][:, 0:EMBED].rearrange("p (k s) -> p k s", k=KC)).then_inc(x_c, 1)

            def h_copy(i, r):
                act.wait_ge(h_mm, i + 1)
                if not (isinstance(i, int) and i < 2):
                    act.wait_ge(h_t, i - 1)
                a.activation(hr[r % 2][:, :], psS[r % 2][:, :], ACT.Relu).then_inc(h_c, 1)

            def h_square(i, r):
                act.wait_ge(h_t, i + 1)
                if not (isinstance(i, int) and i < 2):
                    act.wait_ge(y_mm, i - 1)
                a.activation(hT[r % 2][:, :, :], psT[r % 2][:, :].rearrange("p (j s) -> p j s", s=P), ACT.Square).then_inc(h_sq, 1)

            rolled(act, ((x_copy, 2), (h_copy, 1), (h_square, 0)), 2)

        @block.tensor
        def _(pe):
            mm = nc.tensor.matmul
            pe.wait_ge(made, MADE)
            pe.wait_ge(selected, 1)
            b = selb[:, :, :].rearrange("p e c -> p (e c)")
            mm(loc[:, 0:E * G], before_b[:, :], b, start=True, stop=True)
            mm(cnt[:, 0:E * G], ones_b[:, :], b, start=True, stop=True).then_inc(counted, 1)
            for n in range(NPAIR):
                pe.wait_ge(pair_ready, n + 1)
                ins = mm(acc[:, 0:2 * S], row_hot[n % 4][:, :], entry[n % 4][:, :, :].rearrange("p w s -> p (w s)"),
                         start=n == 0, stop=n == NPAIR - 1).then_inc(pair_used, 1)
            pe.wait_ge(placed, 1)

            def turn(i, r):
                return i // RING if isinstance(i, int) else (i - r) // RING

            def x_transpose(i, r):
                pe.wait_ge(gathered[r], 16 * (turn(i, r) + 1))
                if not (isinstance(i, int) and i < 2):
                    pe.wait_ge(x_c, i - 1)
                for k in range(KC):
                    ins = nc.tensor.transpose(psG[r % 2][:, k * P:(k + 1) * P], xg[r][:, k * P:(k + 1) * P], ident[:, :])
                ins.then_inc(x_t, 1)

            def places(i):
                return [pe.value_load(off_i[0:1, bass.ds(i, 1), s], min_val=0, max_val=ZERO_OFF) for s in range(2)]

            def up(i, r):
                at = places(i)
                pe.wait_ge(x_c, i + 1)
                if not (isinstance(i, int) and i < 2):
                    pe.wait_ge(h_c, i - 1)
                for s, o in enumerate(at):
                    for k in range(KC):
                        ins = mm(psS[r % 2][:, s * UNIT:(s + 1) * UNIT], xgT[r % 2][:, k, :],
                                 w1[:, k, bass.ds(o, UNIT)], start=k == 0, stop=k == KC - 1)
                ins.then_inc(h_mm, 1)

            def h_transpose(i, r):
                pe.wait_ge(h_c, i + 1)
                if not (isinstance(i, int) and i < 2):
                    pe.wait_ge(h_sq, i - 1)
                for j in range(WIDE // P):
                    ins = nc.tensor.transpose(psT[r % 2][:, j * P:(j + 1) * P], hr[r % 2][:, j * P:(j + 1) * P], ident[:, :])
                ins.then_inc(h_t, 1)

            w2_flat = w2[:, :, :].rearrange("p j d -> p (j d)")

            def down(i, r):
                at = places(i)
                pe.wait_ge(h_sq, i + 1)
                if not (isinstance(i, int) and i < 2):
                    pe.wait_ge(y_c, i - 1)
                for s, o in enumerate(at):
                    for j in range(2):
                        ins = mm(psO[r % 2][:, 0:EMBED], hT[r % 2][:, 2 * s + j, :],
                                 w2_flat[:, bass.ds(o * 2 + j * EMBED, EMBED)], start=s + j == 0, stop=s + j == 2)
                ins.then_inc(y_mm, 1)

            rolled(pe, ((x_transpose, 2), (up, 1), (h_transpose, 0), (down, -1)), 2)


MADE = 12
CONSTS = 11
ln_at = {s: n for n, s in enumerate(x for x in pe_order() if x[0] == "LNA")}


def kernel(x, txt, L0_tok_W, L0_tok_b, L0_attn_Wq, L0_attn_bq, L0_attn_Wk, L0_attn_bk, L0_attn_Wv, L0_attn_bv,
           L0_ffn_router_w, L0_ffn_w1, L0_ffn_w2):
    import concourse.bacc as bacc
    from concourse.bass_utils import run_bass_kernel_spmd
    arrays = lay_out(x, txt, L0_tok_W, L0_tok_b, L0_attn_Wq, L0_attn_bq, L0_attn_Wk, L0_attn_bk, L0_attn_Wv,
                     L0_attn_bv, L0_ffn_router_w, L0_ffn_w1, L0_ffn_w2)
    nc = bacc.Bacc("TRN2", target_bir_lowering=False, num_devices=1)
    args = [nc.dram_tensor("in_" + n, a.shape, mybir.dt.from_np(a.dtype), kind="ExternalInput").ap()
            for n, a in arrays.items()]
    out = nc.dram_tensor("out_rows", [TOKENS + P, EMBED], F32, kind="ExternalOutput").ap()
    build(nc, *args, out)
    r = run_bass_kernel_spmd(nc, [{"in_" + n: a for n, a in arrays.items()}], core_ids=[0])
    return r.results[0]["out_rows"][0:TOKENS].reshape(BATCH, SEQ, EMBED)


def lay_out(x, txt, W, b, Wq, bq, Wk, bk, Wv, bv, router, w1, w2):
    g = IMAGE // PATCH
    c = np.ascontiguousarray
    x = np.asarray(x).reshape(BATCH, CHANNELS, g, PATCH, g, PATCH).transpose(0, 1, 2, 4, 3, 5)

    def side(w):
        return np.asarray(w).reshape(8, 2, HD, EMBED).transpose(3, 1, 2, 0).reshape(EMBED, EMBED)

    def side_bias(v):
        return c(np.asarray(v).reshape(8, 2, HD).transpose(2, 0, 1).reshape(P, 2))

    return {
        "patches_t": c(x.reshape(IMG_TOKENS, FEATS).T),
        "txt": c(np.asarray(txt)),
        "w_tok": c(np.asarray(W).T),
        "b_tok": c(np.asarray(b).reshape(1, EMBED)),
        "w_qkv": c(np.concatenate([side(Wq), side(Wk), np.asarray(Wv).reshape(EMBED, EMBED).T], axis=1)),
        "b_q": side_bias(bq),
        "b_k": side_bias(bk),
        "b_v": c(np.asarray(bv).reshape(1, EMBED)),
        "w_router": c(np.asarray(router).T),
        "w_1": c(np.asarray(w1)),
        "w_2": c(np.asarray(w2)),
    }
```
